# Optimizing a Trainium2 kernel written in Bass

```python
import numpy as np
import jax
import jax.numpy as jnp

def _softmax(x, axis=-1):
    return jax.nn.softmax(x, axis=axis)

def _gelu(x):
    return jax.nn.gelu(x, approximate=True)

def _silu(x):
    return jax.nn.silu(x)

def _sigmoid(x):
    return jax.nn.sigmoid(x)

def _layernorm(x, axis=-1, eps=1e-05):
    m = jnp.mean(x, axis=axis, keepdims=True)
    v = jnp.var(x, axis=axis, keepdims=True)
    return (x - m) / jnp.sqrt(v + eps)

def _scatter_add(tgt, idx, src, axis=0):
    return tgt.at[idx].add(src)

def _segment_sum(src, seg, n):
    return jax.ops.segment_sum(src, seg, n)
kernel_name = 'mk_adj_ffn_d1_adj_r2_7227b1'

def setup_inputs(seed: int=0):
    np.random.seed(seed)
    _w = jnp.asarray

    def _rec_inputs():
        import jax
        import jax.numpy as jnp
        _gk = jax.random.key(seed)
        x = -0.0002928 + 1 * jax.random.normal(jax.random.fold_in(_gk, 1), (1354, 256), jnp.float32)
        _w = (1.0 + jnp.arange(1354, dtype=jnp.float32)) ** (-0.5)
        _w = _w / _w.mean()
        _pij = jnp.clip(0.00295421 * _w[:, None] * _w[None, :], 0.0, 1.0)
        _a = jax.random.uniform(jax.random.fold_in(_gk, 2), (1354, 1354)) < _pij
        _a = jnp.logical_or(_a, jnp.swapaxes(_a, -1, -2))
        _a = jnp.logical_or(_a, jnp.eye(1354, dtype=bool))
        _af = _a.astype(jnp.float32)
        _af = _af * jax.random.uniform(jax.random.fold_in(_gk, 3), (1354, 1354), jnp.float32, 0.05, 5.41998)
        adj = _af
        return (x, adj)
    x, adj = _rec_inputs()

    def _L0_gnn_setup():
        import jax, jax.numpy as jnp
        import numpy as np
        N = 4096
        D = 256
        key = jax.random.key(seed)
        ks = jax.random.split(key, 6)
        s = 1.0 / np.sqrt(D)
        return {'x': jax.random.normal(ks[0], (N, D), jnp.float32), 'spatial_encoding': jax.random.normal(ks[1], (N, N), jnp.float32), 'edge_encoding': jax.random.normal(ks[2], (N, N), jnp.float32), 'Wq': jax.random.normal(ks[3], (D, D), jnp.float32) * s, 'bq': jnp.zeros((D,), jnp.float32), 'Wk': jax.random.normal(ks[4], (D, D), jnp.float32) * s, 'bk': jnp.zeros((D,), jnp.float32), 'Wv': jax.random.normal(ks[5], (D, D), jnp.float32) * s, 'bv': jnp.zeros((D,), jnp.float32)}
    _L0_gnn_all = _L0_gnn_setup()
    _L0_gnn_in = {k: v for k, v in _L0_gnn_all.items() if k in ('Wq', 'bq', 'Wk', 'bk', 'Wv', 'bv')}
    del _L0_gnn_all

    def _L0_ffn_setup():
        import jax, jax.numpy as jnp
        import numpy as np
        B, S, D = (4, 1024, 256)
        E, H, K = (8, 512, 2)

        def _moe_forward(x, router_w, router_b, w1, b1, wg, bg, wv, bv, w2, b2):
            b, s, d = x.shape
            xf = x.reshape(-1, d)
            T = xf.shape[0]
            scores = xf @ router_w + router_b
            probs = jax.nn.softmax(scores, axis=-1)
            topk_p, topk_i = jax.lax.top_k(probs, K)
            gates = jnp.zeros((T, E), xf.dtype).at[jnp.arange(T)[:, None], topk_i].set(topk_p)
            h = jnp.einsum('td,edh->teh', xf, w1) + b1[None]
            gated = jax.nn.silu(jnp.einsum('teh,ehf->tef', h, wg) + bg[None]) * (jnp.einsum('teh,ehf->tef', h, wv) + bv[None])
            y = jnp.einsum('tef,efd->ted', gated, w2) + b2[None]
            out = jnp.einsum('ted,te->td', y, gates)
            return out.reshape(b, s, d)
        key = jax.random.key(seed)
        ks = jax.random.split(key, 8)
        s_in = 0.02
        return {'x': jax.random.normal(ks[0], (B, S, D), jnp.float32), 'router_w': jax.random.normal(ks[1], (D, E), jnp.float32) * s_in, 'router_b': jnp.zeros((E,), jnp.float32), 'w1': jax.random.normal(ks[2], (E, D, H), jnp.float32) * s_in, 'b1': jnp.zeros((E, H), jnp.float32), 'wg': jax.random.normal(ks[3], (E, H, H), jnp.float32) * s_in, 'bg': jnp.zeros((E, H), jnp.float32), 'wv': jax.random.normal(ks[4], (E, H, H), jnp.float32) * s_in, 'bv': jnp.zeros((E, H), jnp.float32), 'w2': jax.random.normal(ks[5], (E, H, D), jnp.float32) * s_in, 'b2': jnp.zeros((E, D), jnp.float32)}
    _L0_ffn_all = _L0_ffn_setup()
    _L0_ffn_in = {k: v for k, v in _L0_ffn_all.items() if k in ('router_w', 'router_b', 'w1', 'b1', 'wg', 'bg', 'wv', 'bv', 'w2', 'b2')}
    del _L0_ffn_all
    return {'x': x, 'adj': adj, 'L0_gnn_Wq': _L0_gnn_in['Wq'], 'L0_gnn_bq': _L0_gnn_in['bq'], 'L0_gnn_Wk': _L0_gnn_in['Wk'], 'L0_gnn_bk': _L0_gnn_in['bk'], 'L0_gnn_Wv': _L0_gnn_in['Wv'], 'L0_gnn_bv': _L0_gnn_in['bv'], 'L0_ffn_router_w': _L0_ffn_in['router_w'], 'L0_ffn_router_b': _L0_ffn_in['router_b'], 'L0_ffn_w1': _L0_ffn_in['w1'], 'L0_ffn_b1': _L0_ffn_in['b1'], 'L0_ffn_wg': _L0_ffn_in['wg'], 'L0_ffn_bg': _L0_ffn_in['bg'], 'L0_ffn_wv': _L0_ffn_in['wv'], 'L0_ffn_bv': _L0_ffn_in['bv'], 'L0_ffn_w2': _L0_ffn_in['w2'], 'L0_ffn_b2': _L0_ffn_in['b2']}

def reference(x, adj, L0_gnn_Wq, L0_gnn_bq, L0_gnn_Wk, L0_gnn_bk, L0_gnn_Wv, L0_gnn_bv, L0_ffn_router_w, L0_ffn_router_b, L0_ffn_w1, L0_ffn_b1, L0_ffn_wg, L0_ffn_bg, L0_ffn_wv, L0_ffn_bv, L0_ffn_w2, L0_ffn_b2):
    import jax
    import jax.numpy as jnp

    def _L0_gnn_ref(x, spatial_encoding, edge_encoding, Wq, bq, Wk, bk, Wv, bv):
        import jax, jax.numpy as jnp
        import numpy as np
        N = 4096
        D = 256
        q = x @ Wq.T + bq
        k = x @ Wk.T + bk
        v = x @ Wv.T + bv
        scale = 1.0 / jnp.sqrt(jnp.asarray(q.shape[-1], q.dtype))
        a = q @ k.T * scale + spatial_encoding + edge_encoding
        attn = jax.nn.softmax(a, axis=-1)
        return attn @ v

    def _L0_ffn_ref(x, router_w, router_b, w1, b1, wg, bg, wv, bv, w2, b2):
        import jax, jax.numpy as jnp
        import numpy as np
        B, S, D = (4, 1024, 256)
        E, H, K = (8, 512, 2)

        def _moe_forward(x, router_w, router_b, w1, b1, wg, bg, wv, bv, w2, b2):
            b, s, d = x.shape
            xf = x.reshape(-1, d)
            T = xf.shape[0]
            scores = xf @ router_w + router_b
            probs = jax.nn.softmax(scores, axis=-1)
            topk_p, topk_i = jax.lax.top_k(probs, K)
            gates = jnp.zeros((T, E), xf.dtype).at[jnp.arange(T)[:, None], topk_i].set(topk_p)
            h = jnp.einsum('td,edh->teh', xf, w1) + b1[None]
            gated = jax.nn.silu(jnp.einsum('teh,ehf->tef', h, wg) + bg[None]) * (jnp.einsum('teh,ehf->tef', h, wv) + bv[None])
            y = jnp.einsum('tef,efd->ted', gated, w2) + b2[None]
            out = jnp.einsum('ted,te->td', y, gates)
            return out.reshape(b, s, d)
        return _moe_forward(x, router_w, router_b, w1, b1, wg, bg, wv, bv, w2, b2)
    x = x + _L0_gnn_ref(_layernorm(x, axis=-1), adj, adj, L0_gnn_Wq, L0_gnn_bq, L0_gnn_Wk, L0_gnn_bk, L0_gnn_Wv, L0_gnn_bv)
    x = x + _L0_ffn_ref(_layernorm(x, axis=-1)[None], L0_ffn_router_w, L0_ffn_router_b, L0_ffn_w1, L0_ffn_b1, L0_ffn_wg, L0_ffn_bg, L0_ffn_wv, L0_ffn_bv, L0_ffn_w2, L0_ffn_b2)[0]
    return x

_drawn_inputs = setup_inputs


def setup_inputs(seed=0):
    import zlib

    import numpy as np

    out = dict(_drawn_inputs(seed))
    spreads = {'L0_gnn_bq': (0.0, 0.283),
     'L0_gnn_bk': (0.0, 0.8),
     'L0_gnn_bv': (0.0, 0.1),
     'L0_ffn_router_b': (0.0, 0.8),
     'L0_ffn_b1': (0.0, 0.8),
     'L0_ffn_bg': (0.0, 0.8),
     'L0_ffn_bv': (0.0, 0.8),
     'L0_ffn_b2': (0.0, 0.372)}
    factors = {'L0_ffn_router_w': 3.081,
     'L0_ffn_w1': 8.0,
     'L0_ffn_wg': 8.0,
     'L0_ffn_wv': 8.0,
     'L0_ffn_w2': 8.0}
    for name, (base, spread) in spreads.items():
        noise = np.random.default_rng([zlib.crc32(name.encode()), seed]).standard_normal(out[name].shape)
        drawn = base * np.exp(spread * noise) if base else spread * noise
        out[name] = jnp.asarray(drawn.astype(out[name].dtype))
    for name, factor in factors.items():
        out[name] = (out[name] * factor).astype(out[name].dtype)
    return out
```

```python
from contextlib import ExitStack

import concourse.bass as bass
from concourse import mybir

P = 128
ALU = mybir.AluOpType
ACT = mybir.ActivationFunctionType
AX_X = mybir.AxisListType.X
F32 = mybir.dt.float32
F32R = mybir.dt.float32r
BF16 = mybir.dt.bfloat16
I32 = mybir.dt.int32
U32 = mybir.dt.uint32
EPS = 1e-5
BANK = 512


def known(t, n):
    return not isinstance(t, int) or 0 <= t < n


def wait(eng, sem, value):
    if not isinstance(value, int) or value > 0:
        eng.wait_ge(sem, value)


def wait_apart(eng, passed, *waits):
    for sem, value in waits:
        wait(eng, sem, value)
    if any(not isinstance(value, int) for _, value in waits):
        eng.sem_inc(passed)


def pipeline(eng, step, first, last, total):
    for s in range(first):
        step(s)
    with eng.Fori(first, last) as s:
        step(s)
    for s in range(last, total):
        step(s)


def attention_then_top2_experts(
    nc, x, adj, Wq, bq, Wk, bk, Wv, bv, router_w, router_b, w1, b1, wg, bg, wv, bvv, w2, b2, out
):
    N, D = x.shape
    E, _, H = w1.shape
    TOPK = 2
    TILES = -(-N // P)
    LAST = N - (TILES - 1) * P
    KD, KH = D // P, H // P
    REGION = TILES * P + P
    BLOCKS = (TOPK * N + E - 1 + E * (P - 1)) // P
    SLOTS = 2
    SIZES = [KD * H, KH * H, KH * H, KH * D]
    AT = [sum(SIZES[:i]) for i in range(4)]
    W_SIZE = sum(SIZES)
    B_SIZES = [H, H, H, D]
    B_AT = [sum(B_SIZES[:i]) for i in range(4)]
    B_SIZE = sum(B_SIZES)
    B_SLOTS = 3
    COLS = [H, H, H, D]
    CHUNKS = [(c, min(BANK, N - c)) for c in range(0, N, BANK)]
    PER = BANK // P
    GROUPS = [(g, min(PER, TILES - g)) for g in range(0, TILES, PER)]
    SCALE = float(D) ** -0.5

    def width(t):
        return LAST if isinstance(t, int) and t == TILES - 1 else P

    def span(t, n):
        return slice(t * P, t * P + n) if isinstance(t, int) else bass.ds(t * P, n)

    with ExitStack() as ctx:
        def sem(name):
            return ctx.enter_context(nc.semaphore(name))

        def at(row, i):
            return row[:, i:i + 1] if isinstance(i, int) else row[:, bass.ds(i, 1)]

        def tile_of(buf, i, n):
            return (buf[:n, i, :] if isinstance(i, int) else
                    buf[:n, bass.ds(i, 1), :].rearrange("p a n -> p (a n)"))

        base, top = -(-nc.sbuf_base // 32) * 32, nc.sbuf_usable_end

        class Area:
            def __init__(self, at, end):
                self.at, self.end = at, end

            def place(self, name, shape, dt=F32):
                size = 2 if dt == BF16 else 4
                for s in shape[1:]:
                    size *= s
                t = nc.alloc_sbuf_tensor_at(name, shape, dt, offset=self.at)
                self.at += -(-size // 32) * 32
                assert self.at <= self.end, (name, self.at, self.end)
                return t

        SLOT_BYTES = 2 * W_SIZE * 4
        weights = Area(base, top).place("weights", [P, SLOTS, 2 * W_SIZE], F32R)
        keep = Area(base + SLOTS * SLOT_BYTES, top)
        staged_at = keep.at
        staged = keep.place("staged", [P, W_SIZE])
        xn2_at = keep.at
        xn2_all = keep.place("xn2_all", [P, TILES, D])
        x1 = keep.place("x1", [P, TILES, D])
        bias = keep.place("bias", [P, B_SLOTS, B_SIZE])
        ident = keep.place("ident", [P, P])
        tri = keep.place("tri", [P, P], BF16)
        ones = keep.place("ones", [P, P], BF16)
        zeros = keep.place("zeros", [P, D])
        rw = keep.place("rw", [P, KD, E])
        rb = keep.place("rb", [P, E])
        iota8 = keep.place("iota8", [P, E])
        region_base = keep.place("region_base", [P, E])
        scores_all = keep.place("scores_all", [P, TILES, E])
        scores = keep.place("scores", [P, E])
        top8 = keep.place("top8", [P, E])
        hot_all = keep.place("hot_all", [P, TILES, TOPK, E])
        pos_all = keep.place("pos_all", [P, TILES, TOPK])
        posi_all = keep.place("posi_all", [P, TILES, TOPK], I32)
        top_idx = keep.place("top_idx", [P, E], U32)
        top_idxf = keep.place("top_idxf", [P, TOPK])
        pair = keep.place("pair", [P, TOPK])
        chosen = keep.place("chosen", [P, E], BF16)
        counted = keep.place("counted", [P, E], BF16)
        place_in = keep.place("place_in", [P, E])
        hot_place = keep.place("hot_place", [P, TOPK, E])
        mv = keep.place("mv", [P, TILES, 2])
        rs = keep.place("rs", [P, 6, TILES])
        st2 = keep.place("st2", [P, 6])
        mv2 = keep.place("mv2", [P, 2])
        ln2 = keep.place("ln2", [P, 4])
        gate_e = keep.place("gate_e", [P, TILES, E])
        gate_s = keep.place("gate_s", [P, 3, TILES])
        gates = keep.place("gates", [P, TOPK, TILES])
        negmax = keep.place("negmax", [P, 1])
        rowmax = keep.place("rowmax", [P, 1])
        rowsum = keep.place("rowsum", [P, 1])
        rowinv = keep.place("rowinv", [P, 1])
        count = keep.place("count", [P, 8, E])
        block_row = keep.place("block_row", [P, 32], I32)
        step_experts = keep.place("step_experts", [P, BLOCKS + 4, 4], I32)
        thresholds = keep.place("thresholds", [P, E, TILES])
        block_no = keep.place("block_no", [P, 32])
        up_to = keep.place("up_to", [P, E, E])
        table8 = keep.place("table8", [P, 2, E], I32)
        ypos_i = keep.place("ypos_i", [P, TILES, TOPK], I32)
        bqk = keep.place("bqk", [P, 2, KD])
        moe_at = keep.at

        mid = Area(base + SLOT_BYTES, base + SLOTS * SLOT_BYTES)
        kT = [mid.place(f"kT_{s}", [P, KD, N], F32R) for s in ("hi", "lo")]
        adj_sb = mid.place("adj_sb", [P, N])
        wT = {n: [mid.place(f"w{n}T_{s}", [P, KD, D], F32R) for s in ("hi", "lo")] for n in "qkv"}
        high = Area(moe_at, top)
        v = high.place("v", [P, TILES, 2, D], F32R)
        qT = high.place("qT", [P, KD, N])
        qs = [high.place(f"qs_{s}", [P, KD, P], F32R) for s in ("hi", "lo")]
        xT = [mid.place(f"xT_{s}", [P, KD, BANK], F32R) for s in ("hi", "lo")]
        early = Area(xn2_at, xn2_at + TILES * D * 4)
        wraw = early.place("wraw", [P, 3, KD, D])
        xn = early.place("xn", [P, 2, D])
        bv_row = mid.place("bv_row", [P, D])
        stats = mid.place("stats", [P, TILES, 6])
        ktmp = [(early, high)[m].place(f"ktmp{m}", [P, BANK]) for m in range(KD)]
        vtmp = [(early, high)[m].place(f"vtmp{m}", [P, D]) for m in range(2)]
        late = Area(staged_at, staged_at + W_SIZE * 4)
        probs = late.place("probs", [P, N])
        pT = [late.place(f"pT_{s}", [P, TILES, P], F32R) for s in ("hi", "lo")]
        xn2 = late.place("xn2", [P, D])
        xn2T = late.place("xn2T", [P, KD, P])
        mixed = late.place("mixed", [P, D])
        after = Area(moe_at, top)
        over = after.place("over", [P, E, TILES])
        spread = after.place("spread", [P, E, E])
        block_f = after.place("block_f", [P, 3, 32])
        passed = after.place("passed", [P, 2, 32, E])
        hot_delta = after.place("hot_delta", [P, TILES * TOPK, E])
        gate_h = after.place("gate_h", [P, TILES, E])
        moe = Area(after.at, top)
        xblk, xfirst = moe.place("xblk", [P, D]), moe.place("xfirst", [P, D])
        bT = [moe.place(f"bT_{s}", [P, KD, P], F32R) for s in ("hi", "lo")]
        hsum = moe.place("hsum", [P, H])
        hT = [moe.place(f"hT_{s}", [P, KH, P], F32R) for s in ("hi", "lo")]
        gsum = moe.place("gsum", [P, H])
        silu = moe.place("silu", [P, H])
        vsum = moe.place("vsum", [P, H])
        gated = moe.place("gated", [P, H])
        gT = [moe.place(f"gT_{s}", [P, KH, P], F32R) for s in ("hi", "lo")]
        yhalf = moe.place("yhalf", [P, D])
        ysum = moe.place("ysum", [P, D])
        final = Area(base, staged_at)
        result = final.place("result", [P, TILES, D])
        picked = Area(staged_at, staged_at + 4 * (W_SIZE + TILES * D)).place("picked", [P, TILES, TOPK, D])

        ps = ctx.enter_context(nc.psum_tensor("ps", [P, 8, BANK], F32))
        flat = ps[:, :, :].rearrange("p b n -> p (b n)")

        xs = nc.dram_tensor("expert_rows", [E * REGION, D], F32, kind="Internal").ap()
        biases = nc.dram_tensor("biases", [E, B_SIZE], F32, kind="Internal").ap()
        ys = nc.dram_tensor("expert_out", [BLOCKS * P, D], F32, kind="Internal").ap()

        x_in = [sem(f"x_in{g}") for g in range(len(GROUPS))]
        w_in, small_in, adj_in = sem("w_in"), sem("small_in"), sem("adj_in")
        bias_rows_in, bias_in = sem("bias_rows_in"), sem("bias_in")
        first_in = [sem(f"first_in{p}") for p in range(4)]
        staged_in = [sem(f"staged_in{p}") for p in range(4)]
        hi_in = [sem(f"hi_in{p}") for p in range(4)]
        split_lo = sem("split_lo")
        cleared, dve_passed, pool_passed = sem("cleared"), sem("dve_passed"), sem("pool_passed")
        zeros_set, consts, iotas = sem("zeros_set"), sem("consts"), sem("iotas")
        stat_done, mv_done, newton1 = sem("stat_done"), sem("mv_done"), sem("newton1")
        xn_done, xnT_done, xT_hi, xT_lo = sem("xn_done"), sem("xnT_done"), sem("xT_hi"), sem("xT_lo")
        wT_mm, wT_hi, wT_lo = sem("wT_mm"), sem("wT_hi"), sem("wT_lo")
        v_mm, v_sum, v_hi, v_lo = sem("v_mm"), sem("v_sum"), sem("v_hi"), sem("v_lo")
        k_mm, k_sum, k_hi, k_lo = sem("k_mm"), sem("k_sum"), sem("k_hi"), sem("k_lo")
        bq_done, q_mm, q_sum, q_hi, q_lo = (
            sem("bq_done"), sem("q_mm"), sem("q_sum"), sem("q_hi"), sem("q_lo"))
        scores_mm, logits_done, negmax_done, exp_done = (
            sem("scores_mm"), sem("logits_done"), sem("negmax_done"), sem("exp_done"))
        pT_mm, pT_hi, pT_lo = sem("pT_mm"), sem("pT_hi"), sem("pT_lo")
        mix_mm, mix_half, mix_sum, inv_done, x1_done = (
            sem("mix_mm"), sem("mix_half"), sem("mix_sum"), sem("inv_done"), sem("x1_done"))
        st2_done, mv2_done, var_done, rough_done, newton2 = (
            sem("st2_done"), sem("mv2_done"), sem("var_done"), sem("rough_done"), sem("newton2"))
        xn2_done, xn2_copied = sem("xn2_done"), sem("xn2_copied")
        xn2T_mm, xn2T_done, router_mm = sem("xn2T_mm"), sem("xn2T_done"), sem("router_mm")
        rscore, rkept, rmax, ridx, ridxf, rpair, hot, chosen_done = (
            sem("rscore"), sem("rkept"), sem("rmax"), sem("ridx"), sem("ridxf"), sem("rpair"),
            sem("hot"), sem("chosen_done"))
        rank_mm, rank_sum, rank_hot, pos_done, posi_done, counted_done = (
            sem("rank_mm"), sem("rank_sum"), sem("rank_hot"), sem("pos_done"), sem("posi_done"),
            sem("counted_done"))
        scattered, total_mm, tab = sem("scattered"), sem("total_mm"), sem("tab")
        ends_done, rows_done, experts_set, tables_done = (
            sem("ends_done"), sem("rows_done"), sem("experts_set"), sem("tables_done"))
        ys_cleared, padded, first_rows_in, rows_in = sem("ys_cleared"), sem("padded"), sem("first_rows_in"), sem("rows_in")
        bT_mm, bT_hi, bT_lo = sem("bT_mm"), sem("bT_hi"), sem("bT_lo")
        h_mm, h_sum, hT_mm, hT_hi, hT_lo = (
            sem("h_mm"), sem("h_sum"), sem("hT_mm"), sem("hT_hi"), sem("hT_lo"))
        g_mm, g_sum, silu_done = sem("g_mm"), sem("g_sum"), sem("silu_done")
        u_mm, u_sum, gated_done = sem("u_mm"), sem("u_sum"), sem("gated_done")
        gT_mm, gT_hi, gT_lo = sem("gT_mm"), sem("gT_hi"), sem("gT_lo")
        y_mm, y_lower, y_sum, y_out = sem("y_mm"), sem("y_lower"), sem("y_sum"), sem("y_out")
        gate_in, gate_exp = sem("gate_in"), sem("gate_exp")
        gathered = [[sem(f"gathered{t}_{k}") for k in range(TOPK)] for t in range(TILES)]
        part_added, added, result_out = sem("part_added"), sem("added"), sem("result_out")

        def r32(ap):
            return ap.bitcast(F32)

        def experts_of(engine, s):
            i = s + 2
            row = (step_experts[0:1, i, :] if isinstance(i, int) else
                   step_experts[0:1, bass.ds(i, 1), :].rearrange("p a n -> p (a n)"))
            return nc.values_load_multi_w_load_instructions(row, engines=[engine], min_val=0, max_val=E - 1)[1]

        def matrix(e, p, s):
            w = tile_of(weights[:, :, 2 * AT[p]:2 * (AT[p] + SIZES[p])], e % SLOTS, P)
            return w.rearrange("p (k s n) -> p k s n", s=2, n=COLS[p])[:, :, s, :]

        def staging(p):
            return staged[:, AT[p]:AT[p] + SIZES[p]].rearrange("p (k n) -> p k n", n=COLS[p])

        def source(e, p):
            w = (w1, wg, wv, w2)[p]
            w = w[e] if isinstance(e, int) else w[bass.ds(e, 1), :, :].rearrange("a k n -> (a k) n")
            return w.rearrange("(k p) n -> p k n", p=P)

        def load_bias(pool, e):
            src = biases[e:e + 1, :] if isinstance(e, int) else biases[bass.ds(e, 1), :]
            pool.dma_start(tile_of(bias, e % B_SLOTS, P), src.broadcast_to([P, B_SIZE])).then_inc(bias_in, 16)

        NEWTON2 = 7

        def newton(wait_ge, engine, t, n):
            var, y, tmp = ln2[:n, 0:1], ln2[:n, 1:2], ln2[:n, 2:3]
            wait_ge(rough_done, t + 1)
            engine.tensor_scalar(var, var, -0.5, None, ALU.mult).then_inc(newton2, 1)
            for i in range(3):
                wait_ge(newton2, NEWTON2 * t + 2 * i + 1)
                engine.tensor_scalar(tmp, y, y, var, ALU.mult, ALU.mult).then_inc(newton2, 1)
                wait_ge(newton2, NEWTON2 * t + 2 * i + 2)
                engine.tensor_scalar(y, tmp, 1.5, y, ALU.add, ALU.mult).then_inc(newton2, 1)

        def clear_ends(eng, engine, first):
            ends = nc.values_load_multi_w_load_instructions(
                table8[0:1, 0, first:first + E // 2], engines=[engine], min_val=0, max_val=E * REGION - P)[1]
            for row in ends:
                eng.dma_start(xs[bass.ds(row, P), :], zeros[:, :]).then_inc(padded, 16)

        PASSES = ((1, 0), (0, 1), (0, 0))

        block = ctx.enter_context(nc.Block())
        n_small = [0]

        @block.sync
        def _(sp):
            def load_small(dst, src):
                n_small[0] += 16
                with nc.allow_non_contiguous_dma("biases"):
                    sp.dma_start(dst, src).then_inc(small_in, 16)

            def load_adj(t):
                n = width(t)
                sp.dma_start(adj_sb[:n, :], adj[span(t, n), :]).then_inc(adj_in, 16)

            for g, (t0, n) in enumerate(GROUPS):
                whole = n if t0 + n < TILES else n - 1
                sp.dma_start(x1[:, t0:t0 + whole, :],
                             x[t0 * P:(t0 + whole) * P, :].rearrange("(t p) d -> p t d", p=P)
                             ).then_inc(x_in[g], 16)
            sp.dma_start(x1[:LAST, TILES - 1, :], x[(TILES - 1) * P:N, :]).then_inc(x_in[-1], 16)
            for n, w in enumerate((Wq, Wk, Wv)):
                sp.dma_start(wraw[:, n, :, :], w.rearrange("(k p) d -> p k d", p=P)).then_inc(w_in, 16)
            load_small(bqk[:, 0, :], bq.rearrange("(k p) -> p k", p=P))
            load_small(bqk[:, 1, :], bk.rearrange("(k p) -> p k", p=P))
            load_small(bv_row[:, :], bv.rearrange("(a n) -> a n", a=1).broadcast_to([P, D]))
            load_small(rb[:, :], router_b.rearrange("(a n) -> a n", a=1).broadcast_to([P, E]))
            load_small(rw[:, :, :], router_w.rearrange("(k p) e -> p k e", p=P))
            for p, b in enumerate((b1, bg, bvv, b2)):
                sp.dma_start(biases[:, B_AT[p]:B_AT[p] + B_SIZES[p]], b).then_inc(bias_rows_in, 16)
            load_adj(0)
            for p, w in enumerate((w1, wg, wv, w2)):
                sp.dma_start(staged[:, AT[p]:AT[p] + SIZES[p]].rearrange("p (k n) -> p k n", n=w.shape[2]),
                             w[0].rearrange("(k p) n -> p k n", p=P)).then_inc(first_in[p], 16)

            sp.wait_ge(consts, 4)
            for b in range(BLOCKS):
                sp.dma_start(ys[b * P:(b + 1) * P, :], zeros[:, :]).then_inc(ys_cleared, 16)

            def ahead(s):
                if known(s + 1, TILES):
                    wait(sp, logits_done, s + 1)
                    load_adj(s + 1)
            pipeline(sp, ahead, 0, TILES - 2, TILES)

            def load_staged(e, p):
                if not (isinstance(e, int) and e == 1):
                    wait(sp, split_lo, 4 * (e - 1) + p + 1)
                sp.dma_start(staging(p), source(e, p)).then_inc(staged_in[p], 16)

            sp.wait_ge(mix_mm, TILES)
            for p in (0, 1, 3):
                load_staged(1, p)
            sp.wait_ge(router_mm, TILES)
            load_staged(1, 2)

            sp.wait_ge(ends_done, 1)
            clear_ends(sp, mybir.EngineType.SP, 0)

            with sp.Fori(SLOTS, E) as e:
                for p in range(4):
                    load_staged(e, p)

            for t0, n in GROUPS:
                whole = n if t0 + n < TILES else n - 1
                sp.wait_ge(added, t0 + whole)
                sp.dma_start(out[t0 * P:(t0 + whole) * P, :].rearrange("(t p) d -> p t d", p=P),
                             result[:, t0:t0 + whole, :]).then_inc(result_out, 16)
            sp.wait_ge(added, TILES)
            sp.dma_start(out[(TILES - 1) * P:N, :], result[:LAST, TILES - 1, :]).then_inc(result_out, 16)
            sp.wait_ge(result_out, 16 * (len(GROUPS) + 1))

        @block.gpsimd
        def _(pool):
            nc.gpsimd.memset(ident[:, :], 0.0).then_inc(zeros_set, 1)
            nc.gpsimd.memset(tri[:, :], 1.0).then_inc(zeros_set, 1)
            nc.gpsimd.memset(ones[:, :], 1.0).then_inc(consts, 1)
            nc.gpsimd.memset(zeros[:, :], 0.0).then_inc(consts, 1)
            pool.wait_ge(zeros_set, 2)
            nc.gpsimd.affine_select(out=ident[:, :], in_=ident[:, :], compare_op=ALU.not_equal, fill=1.0,
                                    base=0, pattern=[[-1, P]], channel_multiplier=1).then_inc(consts, 1)
            nc.gpsimd.affine_select(out=tri[:, :], in_=tri[:, :], compare_op=ALU.is_gt, fill=0.0,
                                    base=0, pattern=[[1, P]], channel_multiplier=-1).then_inc(consts, 1)
            nc.gpsimd.iota(iota8[:, :], pattern=[[1, E]], base=0, channel_multiplier=0,
                           allow_small_or_imprecise_dtypes=True).then_inc(iotas, 1)
            nc.gpsimd.iota(region_base[:, :], pattern=[[REGION, E]], base=0, channel_multiplier=0,
                           allow_small_or_imprecise_dtypes=True).then_inc(iotas, 1)

            nc.gpsimd.iota(thresholds[:, :, :], pattern=[[0, E], [P, TILES]], base=0, channel_multiplier=0,
                           allow_small_or_imprecise_dtypes=True).then_inc(iotas, 1)
            nc.gpsimd.iota(block_no[:, :], pattern=[[1, 32]], base=0, channel_multiplier=0,
                           allow_small_or_imprecise_dtypes=True).then_inc(iotas, 1)
            nc.gpsimd.memset(up_to[:, :, :], 1.0).then_inc(zeros_set, 1)
            pool.wait_ge(zeros_set, 3)
            nc.gpsimd.affine_select(out=up_to[:, :, :], in_=up_to[:, :, :], compare_op=ALU.is_ge, fill=0.0,
                                    base=0, pattern=[[1, E], [-1, E]], channel_multiplier=0).then_inc(iotas, 1)

            def load_hi(e, p):
                pool.dma_start(matrix(e, p, 0), source(e, p)).then_inc(hi_in[p], 16)

            def make_lo(e, p):
                if isinstance(e, int) and e == 0:
                    pool.wait_ge(first_in[p], 16)
                else:
                    pool.wait_ge(staged_in[p], 16 * e)
                pool.wait_ge(hi_in[p], 16 * (e + 1))
                nc.gpsimd.tensor_tensor(matrix(e, p, 1), staging(p), r32(matrix(e, p, 0)), ALU.subtract
                                        ).then_inc(split_lo, 1)

            pool.wait_ge(small_in, n_small[0])
            for p in range(4):
                load_hi(0, p)
            pool.wait_ge(bias_rows_in, 64)
            for p in range(4):
                make_lo(0, p)
                if p < B_SLOTS:
                    if p > 0:
                        pool.wait_ge(bias_in, 16 * p)
                    load_bias(pool, p)

            G = nc.gpsimd
            for s in range(2, TILES + 4):
                if known(s - 2, TILES - 1):
                    newton(pool.wait_ge, G, s - 2, width(s - 2))
                if known(s - 3, TILES):
                    t = s - 3
                    n = width(t)
                    pool.wait_ge(ridx, t + 1)
                    G.tensor_copy(scores_all[:n, t, :], scores[:n, :]).then_inc(rkept, 1)
                    G.tensor_copy(top_idxf[:n, :], top_idx[:n, 0:TOPK]).then_inc(ridxf, 1)
                    pool.wait_ge(ridxf, t + 1)
                    for k, op in enumerate((ALU.min, ALU.max)):
                        G.tensor_scalar(pair[:n, k:k + 1], top_idxf[:n, 0:1], top_idxf[:n, 1:2], None, op
                                        ).then_inc(rpair, 1)
                    pool.wait_ge(rpair, TOPK * (t + 1))
                    if t == TILES - 1:
                        pool.wait_ge(cleared, 4)
                    for k in range(TOPK):
                        G.tensor_scalar(hot_all[:n, t, k, :], iota8[:n, :], pair[:n, k:k + 1], None,
                                        ALU.is_equal).then_inc(hot, 1)
                    pool.wait_ge(hot, TOPK * (t + 1))
                if known(s - 4, TILES):
                    t = s - 4
                    n = width(t)
                    if t < TILES - 1:
                        pool.wait_ge(rank_mm, t + 1)
                        G.tensor_tensor(counted[:n, :], counted[:n, :], chosen[:n, :], ALU.add
                                        ).then_inc(counted_done, 1)
                if known(s - 3, TILES):
                    t = s - 3
                    n = width(t)
                    pool.wait_ge(counted_done, t + 1)
                    G.tensor_tensor(chosen[:n, :], hot_all[:n, t, 0, :], hot_all[:n, t, 1, :], ALU.add
                                    ).then_inc(chosen_done, 1)
                if known(s - 4, TILES):
                    t = s - 4
                    n = width(t)
                    pool.wait_ge(pos_done, t + 1)
                    G.tensor_copy(posi_all[:n, t, :], pos_all[:n, t, :]).then_inc(posi_done, 1)
                    pool.wait_ge(posi_done, t + 1)
                    for k in range(TOPK):
                        pool.indirect_dma_start(
                            out=xs, out_offset=bass.IndirectOffsetOnAxis(ap=posi_all[:n, t, k:k + 1], axis=0),
                            in_=xn2_all[:n, t, :], in_offset=None).then_inc(scattered, 16)

            for p in range(2):
                load_hi(1, p)
            for p in range(2):
                make_lo(1, p)
            pool.wait_ge(rows_in, 16)
            for p in range(2, 4):
                load_hi(1, p)
            for p in range(2, 4):
                make_lo(1, p)
            pool.wait_ge(tables_done, 1)

            def blocks_before(e):
                return pool.value_load(at(table8[0:1, 1, :], e), min_val=1, max_val=BLOCKS)

            def load_after(mm, done, e, p):
                wait_apart(pool, pool_passed, (mm, done))
                load_hi(e, p)

            def expert(e):
                done = blocks_before(e)
                make_lo(e, 0)
                load_after(u_mm, done, e, 2)
                make_lo(e, 1)
                more = not isinstance(e, int) or e + 1 < E
                if more:
                    done_next = blocks_before(e + 1)
                    load_after(h_mm, done_next, e + 1, 0)
                make_lo(e, 2)
                load_after(y_mm, done, e, 3)
                if more:
                    load_after(g_mm, done_next, e + 1, 1)
                make_lo(e, 3)
                if more:
                    wait_apart(pool, pool_passed, (y_sum, done), (bias_in, 16 * (e + 1)))
                    load_bias(pool, e + 1)
            first_done = blocks_before(SLOTS)
            load_after(h_mm, first_done, SLOTS, 0)
            load_after(g_mm, first_done, SLOTS, 1)
            with pool.Fori(SLOTS, E - 1) as e:
                expert(e)
            expert(E - 1)

            pool.wait_ge(split_lo, 4 * E)
            done = pool.value_load(table8[0:1, 1, 0:1], min_val=1, max_val=BLOCKS)
            for k, need in ((0, 16 * done), (1, 16 * BLOCKS)):
                pool.wait_ge(y_out, need)
                pool.sem_inc(pool_passed)
                for t in range(TILES):
                    n = width(t)
                    pool.indirect_dma_start(
                        out=picked[:n, t, k, :], out_offset=None, in_=ys,
                        in_offset=bass.IndirectOffsetOnAxis(ap=ypos_i[:n, t, k:k + 1], axis=0)
                    ).then_inc(gathered[t][k], 16)

        @block.scalar
        def _(act):
            def copy(o, i):
                return nc.scalar.activation(o, i, ACT.Copy)

            def by_k(ap, k):
                return ap.rearrange("p (k n) -> p k n", k=k)

            def q_part(t):
                n = width(t)
                wait(act, scores_mm, t)
                copy(qs[0][:, :, :n], qT[:, :, span(t, n)]).then_inc(q_hi, 1)

            for n in range(3):
                act.wait_ge(wT_mm, n + 1)
                copy(wT["qkv"[n]][0][:, :, :], by_k(ps[:, 4 + n, :], KD)).then_inc(wT_hi, 1)

            def x_hi(t, c):
                w = width(t)
                act.wait_ge(xnT_done, t + 1)
                copy(xT[0][:, :, c:c + w], by_k(ps[:, t % 2, 0:D], KD)[:, :, 0:w]).then_inc(xT_hi, 1)

            n_k = 0
            for g, (t0, n) in enumerate(GROUPS):
                for t in range(t0, t0 + n):
                    if t == 0 or t > t0:
                        x_hi(t, (t - t0) * P)
                    if t > 0:
                        act.wait_ge(v_sum, t)
                        copy(v[:width(t - 1), t - 1, 0, :], vtmp[(t - 1) % 2][:width(t - 1), :]).then_inc(v_hi, 1)
                if t0 + n == TILES:
                    act.wait_ge(v_sum, TILES)
                    copy(v[:LAST, TILES - 1, 0, :], vtmp[(TILES - 1) % 2][:LAST, :]).then_inc(v_hi, 1)
                cols = slice(t0 * P, min(N, (t0 + n) * P))
                size = cols.stop - cols.start
                for m in range(KD):
                    n_k += 1
                    act.wait_ge(k_mm, n_k)
                    if n_k > KD:
                        act.wait_ge(k_lo, n_k - KD)
                    nc.scalar.activation(ktmp[m][:, 0:size], ps[:, 4 + m, 0:size], ACT.Identity,
                                         bias=bqk[:, 1, m:m + 1]).then_inc(k_sum, 1)
                    act.wait_ge(k_sum, n_k)
                    copy(kT[0][:, m, cols], ktmp[m][:, 0:size]).then_inc(k_hi, 1)
                for m in range(KD):
                    act.wait_ge(bq_done, 1)
                    act.wait_ge(q_mm, n_k - KD + m + 1)
                    nc.scalar.activation(qT[:, m, cols], ps[:, 6 + m, 0:size], ACT.Identity,
                                         bias=bqk[:, 0, m:m + 1], scale=SCALE / 2).then_inc(q_sum, 1)
                    if m == KD - 2 and g + 1 < len(GROUPS):
                        act.wait_ge(q_mm, n_k)
                        x_hi(t0 + n, 0)
                if g == 1:
                    act.wait_ge(q_sum, KD)
                    q_part(0)

            act.wait_ge(q_sum, KD * len(GROUPS))

            def tiles(s):
                if known(s - 3, TILES):
                    t = s - 3
                    n = width(t)
                    wait(act, xn2T_mm, t + 1)
                    wait(act, router_mm, t)
                    copy(xn2T[:, :, :n], by_k(ps[:, 7, 0:D], KD)[:, :, 0:n]).then_inc(xn2T_done, 1)
                if known(s - 1, TILES):
                    t = s - 1
                    n = width(t)
                    for c, (k0, kn) in enumerate(GROUPS):
                        wait(act, pT_mm, len(GROUPS) * t + c + 1)
                        if c == 0:
                            wait(act, mix_mm, t)
                        for rows, ks, kc in ((P, k0, kn if k0 + kn < TILES else kn - 1),
                                             (LAST, TILES - 1, 1 if k0 + kn == TILES else 0)):
                            if kc:
                                o = copy(pT[0][:rows, ks:ks + kc, :n],
                                         ps[:rows, 3 + c, :].rearrange("p (k n) -> p k n", n=P)
                                         [:, ks - k0:ks - k0 + kc, 0:n])
                        o.then_inc(pT_hi, 1)
                if known(s + 1, TILES):
                    q_part(s + 1)
                if known(s - 2, TILES):
                    t = s - 2
                    n = width(t)
                    wait(act, xn2_done, t + 1)
                    wait(act, xn2T_mm, t)
                    copy(xn2[:n, :], tile_of(xn2_all, t, n)).then_inc(xn2_copied, 1)
                if known(s, TILES):
                    t = s
                    n = width(t)
                    wait(act, negmax_done, t + 1)
                    wait(act, inv_done, t)
                    nc.scalar.activation(probs[:n, :], probs[:n, :], ACT.Exp, bias=negmax[:n, :],
                                         accum_out=rowsum[:n, :]).then_inc(exp_done, 1)
            pipeline(act, tiles, 4, TILES - 2, TILES + 3)

            def load_rows(b):
                if isinstance(b, int) and b == 0:
                    buf, done = xfirst, first_rows_in
                else:
                    buf, done = xblk, rows_in
                if not (isinstance(b, int) and b == 1):
                    wait(act, bT_mm, b)
                row = act.value_load(at(block_row[0:1, :], b), min_val=0, max_val=E * REGION - P)
                act.dma_start(buf[:, :], xs[bass.ds(row, P), :]).then_inc(done, 16)

            act.wait_ge(ends_done, 1)
            clear_ends(act, mybir.EngineType.Activation, E // 2)
            act.wait_ge(gate_in, 1)
            nc.scalar.activation(gate_e[:, :, :], gate_e[:, :, :], ACT.Exp).then_inc(gate_exp, 1)
            act.wait_ge(ys_cleared, 16 * BLOCKS)
            act.wait_ge(padded, 16 * E)
            act.wait_ge(rows_done, 1)
            act.wait_ge(scattered, 16 * TOPK * TILES)
            load_rows(0)
            load_rows(1)

            def experts(s):
                if known(s, BLOCKS):
                    wait(act, hT_mm, s + 1)
                    wait(act, u_mm, s)
                    copy(hT[0][:, :, :], by_k(ps[:, 0, :], KH)).then_inc(hT_hi, 1)
                if known(s - 1, BLOCKS):
                    wait(act, gT_mm, s)
                    wait(act, y_mm, s - 1)
                    copy(gT[0][:, :, :], by_k(ps[:, 4, :], KH)).then_inc(gT_hi, 1)
                if known(s + 2, BLOCKS):
                    wait(act, bT_mm, s + 3)
                    wait(act, h_mm, s + 2)
                    copy(bT[0][:, :, :], by_k(ps[:, 6, 0:D], KD)).then_inc(bT_hi, 1)
                if known(s, BLOCKS):
                    wait(act, g_sum, s + 1)
                    wait(act, gated_done, s)
                    nc.scalar.activation(silu[:, :], gsum[:, :], ACT.Silu).then_inc(silu_done, 1)
                if known(s + 3, BLOCKS) and not (isinstance(s, int) and s == -2):
                    load_rows(s + 3)
                if known(s - 2, BLOCKS):
                    wait(act, y_sum, s - 1)
                    act.dma_start(ys[span(s - 2, P), :], ysum[:, :]).then_inc(y_out, 16)
            for s in (-2, -1):
                experts(s)
            pipeline(act, experts, 3, BLOCKS - 3, BLOCKS + 2)

        @block.tensor
        def _(pe):
            def product(o, pairs, inc=None):
                m = [(a[i], b[j]) for a, b in pairs for i, j in PASSES]
                for n, (a, b) in enumerate(m):
                    last = nc.tensor.matmul(o, a, b, start=n == 0, stop=n == len(m) - 1)
                return last

            pe.wait_ge(consts, 4)
            pe.wait_ge(w_in, 48)
            for n in range(3):
                for k in range(KD):
                    for m in range(KD):
                        last = nc.tensor.transpose(ps[:, 4 + n, k * D + m * P:k * D + (m + 1) * P],
                                                   wraw[:, n, m, k * P:(k + 1) * P], ident[:, :])
                last.then_inc(wT_mm, 1)

            n_k = 0

            def both(pair, *index):
                return [buf[index] for buf in pair]

            def transpose_x(t):
                w = width(t)
                pe.wait_ge(xn_done, t + 1)
                if t >= 2:
                    pe.wait_ge(xT_lo, t - 1)
                for k in range(KD):
                    last = nc.tensor.transpose(ps[:, t % 2, k * P:k * P + w],
                                               xn[:w, t % 2, k * P:(k + 1) * P], ident[:w, :w])
                last.then_inc(xnT_done, 1)

            transpose_x(0)
            for g, (t0, n) in enumerate(GROUPS):
                for t in range(t0, t0 + n):
                    w, c = width(t), (t - t0) * P
                    if t + 1 < TILES:
                        transpose_x(t + 1)
                    pe.wait_ge(xT_lo, t + 1)
                    if t == 0:
                        pe.wait_ge(wT_lo, 3)
                    if t >= 2:
                        pe.wait_ge(v_sum, t - 1)
                    product(ps[:w, 2 + t % 2, 0:D],
                            [(both(xT, slice(None), k, slice(c, c + w)), both(wT["v"], slice(None), k, slice(None)))
                             for k in range(KD)]).then_inc(v_mm, 1)
                size = min(N, (t0 + n) * P) - t0 * P
                for name, done, summed in (("k", k_mm, k_sum), ("q", q_mm, q_sum)):
                    for m in range(KD):
                        if g > 0:
                            pe.wait_ge(summed, KD * (g - 1) + m + 1)
                        product(ps[:, (4 if name == "k" else 6) + m, 0:size],
                                [(both(wT[name], slice(None), k, slice(m * P, (m + 1) * P)),
                                  both(xT, slice(None), k, slice(0, size))) for k in range(KD)]
                                ).then_inc(done, 1)

            def scores_of(t):
                n = width(t)
                wait(pe, q_lo, t + 1)
                wait(pe, k_lo, KD * len(GROUPS))
                wait(pe, logits_done, t)
                for c, (k0, kn) in enumerate(CHUNKS):
                    last = product(ps[:n, c, 0:kn],
                                   [(both(qs, slice(None), k, slice(0, n)),
                                     both(kT, slice(None), k, slice(k0, k0 + kn))) for k in range(KD)])
                last.then_inc(scores_mm, 1)

            def tiles(s):
                second = isinstance(s, int) and s == 1
                if second:
                    scores_of(s)
                if known(s - 1, TILES):
                    t = s - 1
                    n = width(t)
                    wait(pe, exp_done, t + 1)
                    wait(pe, pT_lo, len(GROUPS) * t)
                    for c, (k0, kn) in enumerate(GROUPS):
                        for k in range(k0, k0 + kn):
                            w = width(k)
                            last = nc.tensor.transpose(ps[:w, 3 + c, (k - k0) * P:(k - k0) * P + n],
                                                       probs[:n, k * P:k * P + w], ident[:n, :n])
                        last.then_inc(pT_mm, 1)
                if known(s - 3, TILES):
                    t = s - 3
                    n = width(t)
                    wait(pe, xn2T_done, t + 1)
                    wait(pe, rscore, t)
                    for k in range(KD):
                        last = nc.tensor.matmul(ps[:n, 7, 256:256 + E], xn2T[:, k, :n], rw[:, k, :],
                                                start=k == 0, stop=k == KD - 1)
                    last.then_inc(router_mm, 1)
                if known(s, TILES) and not second:
                    scores_of(s)
                if known(s - 4, TILES):
                    t = s - 4
                    n = width(t)
                    if known(s - 3, TILES):
                        wait(pe, rscore, s - 2)
                    wait(pe, chosen_done, t + 1)
                    wait(pe, counted_done, t + 1)
                    wait(pe, rank_sum, t)
                    nc.tensor.matmul(ps[:n, 7, 288:288 + E], tri[:n, :n], chosen[:n, :], start=True, stop=False)
                    nc.tensor.matmul(ps[:n, 7, 288:288 + E], ones[:, :n], counted[:, :], start=False, stop=True
                                     ).then_inc(rank_mm, 1)
                    if isinstance(t, int) and t == TILES - 1:
                        nc.tensor.matmul(ps[:, 7, 320:320 + E], ones[:n, :], chosen[:n, :], start=True, stop=False)
                        nc.tensor.matmul(ps[:, 7, 320:320 + E], ones[:, :], counted[:, :], start=False, stop=True
                                         ).then_inc(total_mm, 1)
                if known(s - 1, TILES):
                    t = s - 1
                    n = width(t)
                    wait(pe, v_lo, TILES)
                    wait(pe, mix_sum, t)
                    for k in range(TILES):
                        c = k // PER
                        if k % PER == 0:
                            wait(pe, pT_lo, len(GROUPS) * t + c + 1)
                        w = width(k)
                        nc.tensor.matmul(ps[:n, 6, :], pT[0][:w, k, :n], v[:w, k, :, :].rearrange("p s n -> p (s n)"),
                                         start=k == 0, stop=False)
                        last = nc.tensor.matmul(ps[:n, 6, 0:D], pT[1][:w, k, :n], v[:w, k, 0, :],
                                                start=False, stop=k == TILES - 1)
                    last.then_inc(mix_mm, 1)
                if known(s - 2, TILES):
                    t = s - 2
                    n = width(t)
                    wait(pe, xn2_copied, t + 1)
                    wait(pe, rank_sum, t - 1)
                    for k in range(KD):
                        last = nc.tensor.transpose(ps[:, 7, k * P:k * P + n], xn2[:n, k * P:(k + 1) * P],
                                                   ident[:n, :n])
                    last.then_inc(xn2T_mm, 1)
            pe.wait_ge(small_in, n_small[0])
            pipeline(pe, tiles, 5, TILES - 2, TILES + 4)
            def split(e, p):
                pe.wait_ge(split_lo, 4 * e + (p + 1))

            def part(e, p, k, s, n):
                c = 2 * AT[p] + (2 * k + s) * COLS[p]
                return weights[:, bass.ds(e % SLOTS, 1), c:c + n].rearrange("p a n -> p (a n)")

            def against(o, stationary, e, p, K):
                m = [(k, i, j) for k in range(K) for i, j in PASSES]
                for n, (k, i, j) in enumerate(m):
                    last = nc.tensor.matmul(o, stationary[i][:, k, :], part(e, p, k, j, COLS[p]),
                                            start=n == 0, stop=n == len(m) - 1)
                return last

            def experts(s):
                e_y, _, e_gv, e_h = experts_of(mybir.EngineType.PE, s)
                if known(s, BLOCKS):
                    wait(pe, h_sum, s + 1)
                    wait(pe, hT_lo, s)
                    for k in range(KH):
                        last = nc.tensor.transpose(ps[:, 0, k * P:(k + 1) * P], hsum[:, k * P:(k + 1) * P],
                                                   ident[:, :])
                    last.then_inc(hT_mm, 1)
                if known(s - 2, BLOCKS):
                    split(e_y, 3)
                    wait(pe, gT_lo, s - 1)
                    wait(pe, y_sum, s - 2)
                    for k in range(KH):
                        nc.tensor.matmul(ps[:, 5, :], gT[0][:, k, :], part(e_y, 3, k, 0, 2 * D),
                                         start=k == 0, stop=False)
                        last = nc.tensor.matmul(ps[:, 5, 0:D], gT[1][:, k, :], part(e_y, 3, k, 0, D),
                                                start=False, stop=k == KH - 1)
                    last.then_inc(y_mm, 1)
                if known(s + 1, BLOCKS):
                    split(e_h, 0)
                    wait(pe, bT_lo, s + 2)
                    wait(pe, h_sum, s + 1)
                    against(ps[:, 1, :], bT, e_h, 0, KD).then_inc(h_mm, 1)
                if known(s - 1, BLOCKS):
                    wait(pe, gated_done, s)
                    wait(pe, gT_lo, s - 1)
                    for k in range(KH):
                        last = nc.tensor.transpose(ps[:, 4, k * P:(k + 1) * P], gated[:, k * P:(k + 1) * P],
                                                   ident[:, :])
                    last.then_inc(gT_mm, 1)
                if known(s, BLOCKS):
                    split(e_gv, 1)
                    wait(pe, hT_lo, s + 1)
                    wait(pe, g_sum, s)
                    against(ps[:, 2, :], hT, e_gv, 1, KH).then_inc(g_mm, 1)
                if known(s + 2, BLOCKS):
                    if isinstance(s, int) and s == -2:
                        pe.wait_ge(first_rows_in, 16)
                    else:
                        wait(pe, rows_in, 16 * (s + 2))
                    wait(pe, bT_lo, s + 2)
                    rows = xfirst if isinstance(s, int) and s == -2 else xblk
                    for k in range(KD):
                        last = nc.tensor.transpose(ps[:, 6, k * P:(k + 1) * P], rows[:, k * P:(k + 1) * P],
                                                   ident[:, :])
                    last.then_inc(bT_mm, 1)
                if known(s, BLOCKS):
                    split(e_gv, 2)
                    wait(pe, u_sum, s)
                    against(ps[:, 3, :], hT, e_gv, 2, KH).then_inc(u_mm, 1)
            pe.wait_ge(experts_set, 4)
            for s in (-2, -1):
                experts(s)
            pipeline(pe, experts, 3, BLOCKS - 2, BLOCKS + 2)

        @block.vector
        def _(dve):
            V = nc.vector

            def sub(o, a, b):
                return V.tensor_tensor(o, a, b, ALU.subtract)

            MAGIC = float(0x5f3759df)

            def rough_rsqrt(y, var):
                return V.tensor_scalar(y.bitcast(I32), var.bitcast(I32), -0.5, MAGIC, ALU.mult, ALU.add)

            def rsqrt(var, half, y, tmp, done, count):
                def step(ins):
                    nonlocal count
                    count = count + 1
                    ins.then_inc(done, 1)
                    wait(dve, done, count)
                step(V.tensor_scalar(half, var, EPS, None, ALU.add))
                step(rough_rsqrt(y, half))
                step(V.tensor_scalar(half, half, -0.5, None, ALU.mult))
                for _ in range(3):
                    step(V.tensor_tensor(tmp, y, y, ALU.mult))
                    step(V.tensor_tensor(tmp, tmp, half, ALU.mult))
                    step(V.scalar_tensor_tensor(y, tmp, 1.5, y, ALU.add, ALU.mult))
            NEWTON = 12

            V.memset(mv[:, :, :], 1.0).then_inc(mv_done, 1)
            V.memset(counted[:, :], 0.0).then_inc(counted_done, 1)
            for buf in (scores_all, hot_all, pos_all):
                V.memset(buf[:, TILES - 1], 0.0).then_inc(cleared, 1)
            V.memset(step_experts[:, :, :], 0).then_inc(cleared, 1)

            def scale_bq():
                dve.wait_ge(small_in, n_small[0])
                V.tensor_scalar(bqk[:, 0, :], bqk[:, 0, :], SCALE / 2, None, ALU.mult).then_inc(bq_done, 1)

            def statistics(g):
                t0, n = GROUPS[g]
                dve.wait_ge(x_in[g], 16 if t0 + n < TILES else 32)
                for t in range(t0, t0 + n):
                    V.bn_stats(stats[:width(t), t, :], x1[:width(t), t, :]).then_inc(stat_done, 1)
                dve.wait_ge(mv_done, t0 + 1)
                for t in range(t0, t0 + n):
                    dve.wait_ge(stat_done, t + 1)
                    V.bn_aggr(mv[:width(t), t, :], stats[:width(t), t, :]).then_inc(mv_done, 1)
                dve.wait_ge(mv_done, t0 + n + 1)

            def normalise(t):
                w = width(t)
                if t >= 2:
                    dve.wait_ge(xnT_done, t - 1)
                V.tensor_scalar(xn[:w, t % 2, :], x1[:w, t, :], mv[:w, t, 0:1], rs[:w, 1, t:t + 1],
                                ALU.subtract, ALU.mult).then_inc(xn_done, 1)

            def v_rows(t):
                w = width(t)
                dve.wait_ge(v_mm, t + 1)
                if t >= 2:
                    dve.wait_ge(v_lo, t - 1)
                V.tensor_tensor(vtmp[t % 2][:w, :], ps[:w, 2 + t % 2, 0:D], bv_row[:w, :], ALU.add
                                ).then_inc(v_sum, 1)

            def v_rest(t):
                w = width(t)
                dve.wait_ge(v_hi, t + 1)
                sub(v[:w, t, 1, :], vtmp[t % 2][:w, :], r32(v[:w, t, 0, :])).then_inc(v_lo, 1)

            def x_rest(t, c):
                w = width(t)
                dve.wait_ge(xT_hi, t + 1)
                sub(xT[1][:, :, c:c + w], ps[:, t % 2, 0:D].rearrange("p (k n) -> p k n", k=KD)[:, :, 0:w],
                    r32(xT[0][:, :, c:c + w])).then_inc(xT_lo, 1)

            def q_rest(t):
                n = width(t)
                wait(dve, q_hi, t + 1)
                sub(qs[1][:, :, :n], qT[:, :, span(t, n)], r32(qs[0][:, :, :n])).then_inc(q_lo, 1)

            for g in range(len(GROUPS)):
                statistics(g)
            rsqrt(mv[:, :, 1], rs[:, 0, :], rs[:, 1, :], rs[:, 2, :], newton1, 0)
            normalise(0)
            normalise(1)
            scale_bq()
            for n in range(3):
                dve.wait_ge(wT_hi, n + 1)
                w = wT["qkv"[n]]
                sub(w[1][:, :, :], ps[:, 4 + n, :].rearrange("p (k n) -> p k n", k=KD), r32(w[0][:, :, :])
                    ).then_inc(wT_lo, 1)
            n_k = 0
            for g, (t0, n) in enumerate(GROUPS):
                for t in range(t0, t0 + n):
                    if t == 0 or t > t0:
                        x_rest(t, (t - t0) * P)
                    if t + 2 < TILES:
                        normalise(t + 2)
                    if t > 0:
                        v_rows(t - 1)
                        if t > 1:
                            v_rest(t - 2)
                if t0 + n == TILES:
                    v_rows(TILES - 1)
                    v_rest(TILES - 2)
                    v_rest(TILES - 1)
                cols = slice(t0 * P, min(N, (t0 + n) * P))
                size = cols.stop - cols.start
                for m in range(KD):
                    n_k += 1
                    dve.wait_ge(k_hi, n_k)
                    sub(kT[1][:, m, cols], ktmp[m][:, 0:size], r32(kT[0][:, m, cols])).then_inc(k_lo, 1)
                if g + 1 < len(GROUPS):
                    x_rest(t0 + n, 0)
                if g == 1:
                    q_rest(0)

            dve.wait_ge(split_lo, 4)

            def tiles(s):
                if known(s - 1, TILES):
                    t = s - 1
                    n = width(t)
                    for c, (k0, kn) in enumerate(GROUPS):
                        wait(dve, pT_hi, len(GROUPS) * t + c + 1)
                        for rows, ks, kc in ((P, k0, kn if k0 + kn < TILES else kn - 1),
                                             (LAST, TILES - 1, 1 if k0 + kn == TILES else 0)):
                            if kc:
                                o = sub(pT[1][:rows, ks:ks + kc, :n],
                                        ps[:rows, 3 + c, :].rearrange("p (k n) -> p k n", n=P)
                                        [:, ks - k0:ks - k0 + kc, 0:n],
                                        r32(pT[0][:rows, ks:ks + kc, :n]))
                        o.then_inc(pT_lo, 1)
                    V.reciprocal(rowinv[:n, :], rowsum[:n, :]).then_inc(inv_done, 1)
                if known(s - 3, TILES):
                    t = s - 3
                    n = width(t)
                    wait(dve, router_mm, t + 1)
                    wait(dve, rkept, t)
                    V.tensor_tensor(scores[:n, :], ps[:n, 7, 256:256 + E], rb[:n, :], ALU.add
                                    ).then_inc(rscore, 1)
                    wait_apart(dve, dve_passed, (rscore, t + 1))
                    V.max(top8[:n, :], scores[:n, :]).then_inc(rmax, 1)
                    wait_apart(dve, dve_passed, (rmax, t + 1), (ridxf, t))
                    V.max_index(top_idx[:n, :], top8[:n, :], scores[:n, :]).then_inc(ridx, 1)
                if known(s - 2, TILES):
                    t = s - 2
                    n = width(t)
                    if isinstance(t, int) and t == TILES - 1:
                        newton(dve.wait_ge, V, t, n)
                    wait(dve, newton2, NEWTON2 * (t + 1))
                    V.tensor_scalar(tile_of(xn2_all, t, n), tile_of(x1, t, n), mv2[:n, 0:1], ln2[:n, 1:2],
                                    ALU.subtract, ALU.mult).then_inc(xn2_done, 1)
                if known(s, TILES):
                    t = s
                    n = width(t)
                    wait_apart(dve, dve_passed, (adj_in, 16 * (t + 1)), (scores_mm, t + 1))
                    V.tensor_tensor_reduce(out=probs[:n, :], in0=flat[:n, 0:N], in1=adj_sb[:n, :],
                                           scale=2.0, scalar=-3.0e38, op0=ALU.add, op1=ALU.max,
                                           accum_out=rowmax[:n, :]).then_inc(logits_done, 1)
                    wait(dve, logits_done, t + 1)
                    V.tensor_scalar(negmax[:n, :], rowmax[:n, :], -1.0, None, ALU.mult).then_inc(negmax_done, 1)
                if known(s - 4, TILES):
                    t = s - 4
                    n = width(t)
                    wait(dve, rank_mm, t + 1)
                    if isinstance(t, int) and t == TILES - 1:
                        dve.wait_ge(total_mm, 1)
                    V.tensor_tensor(place_in[:n, :], ps[:n, 7, 288:288 + E], region_base[:n, :], ALU.add
                                    ).then_inc(rank_sum, 1)
                    wait(dve, rank_sum, t + 1)
                    wait(dve, hot, TOPK * (t + 1))
                    hot_t = (hot_all[:n, t, :, :] if isinstance(t, int) else
                             hot_all[:n, bass.ds(t, 1), :, :].rearrange("p a k e -> p (a k) e"))
                    V.tensor_tensor(hot_place[:n, :, :], hot_t, place_in[:n, :].rearrange("p (a e) -> p a e", a=1)
                                    .broadcast_to([n, TOPK, E]), ALU.mult).then_inc(rank_hot, 1)
                    wait(dve, rank_hot, t + 1)
                    V.tensor_reduce(tile_of(pos_all, t, n), hot_place[:n, :, :], AX_X, ALU.add
                                    ).then_inc(pos_done, 1)
                if known(s + 1, TILES):
                    q_rest(s + 1)
                if known(s - 1, TILES):
                    t = s - 1
                    n = width(t)
                    wait(dve, inv_done, t + 1)
                    wait(dve, mix_mm, t + 1)
                    V.scalar_tensor_tensor(mixed[:n, :], ps[:n, 6, 0:D], rowinv[:n, :], tile_of(x1, t, n),
                                           ALU.mult, ALU.add).then_inc(mix_half, 1)
                    wait(dve, mix_half, t + 1)
                    V.scalar_tensor_tensor(tile_of(x1, t, n), ps[:n, 6, D:2 * D], rowinv[:n, :], mixed[:n, :],
                                           ALU.mult, ALU.add).then_inc(mix_sum, 1)
                    wait_apart(dve, dve_passed, (mix_sum, t + 1))
                    V.bn_stats(st2[:n, :], tile_of(x1, t, n)).then_inc(st2_done, 1)
                    wait_apart(dve, dve_passed, (st2_done, t + 1), (xn2_done, t))
                    V.bn_aggr(mv2[:n, :], st2[:n, :]).then_inc(mv2_done, 1)
                    wait(dve, mv2_done, t + 1)
                    V.tensor_scalar(ln2[:n, 0:1], mv2[:n, 1:2], EPS, None, ALU.add).then_inc(var_done, 1)
                    wait(dve, var_done, t + 1)
                    rough_rsqrt(ln2[:n, 1:2], ln2[:n, 0:1]).then_inc(rough_done, 1)
            dve.wait_ge(iotas, 5)
            pipeline(dve, tiles, 4, TILES - 2, TILES + 4)

            steps = [0]

            def table(ins):
                steps[0] += 1
                ins.then_inc(tab, 1)
                dve.wait_ge(tab, steps[0])

            nblk, upto, weight, ends, shift = (count[:, i, :] for i in range(5))
            last = count[:, 5, 0:1]
            tokens = ps[:, 7, 320:320 + E]
            b, e_of, row = (block_f[:, i, 0:BLOCKS] for i in range(3))
            p0, p1 = passed[:, 0, 0:BLOCKS, :], passed[:, 1, 0:BLOCKS, :]

            def over_blocks(c):
                return c.rearrange("p (a e) -> p a e", a=1).broadcast_to([P, BLOCKS, E])

            def over_experts(c):
                return c.rearrange("p (t a) -> p t a", a=1).broadcast_to([P, TILES, E])
            table(V.tensor_reduce(gate_s[:, 0, :], scores_all[:, :, :], AX_X, ALU.max))
            sub(gate_e[:, :, :], scores_all[:, :, :], over_experts(gate_s[:, 0, :])).then_inc(gate_in, 1)
            V.tensor_tensor(table8[:, 0, :], tokens, region_base[:, :], ALU.add).then_inc(ends_done, 1)
            table(V.tensor_tensor(over[:, :, :], tokens.rearrange("p (e a) -> p e a", a=1).broadcast_to([P, E, TILES]),
                                  thresholds[:, :, :], ALU.is_gt))
            table(V.tensor_reduce(nblk, over[:, :, :], AX_X, ALU.add))
            table(V.tensor_scalar(nblk, nblk, 1.0, None, ALU.max))
            table(V.tensor_tensor(spread[:, :, :], up_to[:, :, :],
                                  nblk.rearrange("p (a e) -> p a e", a=1).broadcast_to([P, E, E]), ALU.mult))
            table(V.tensor_reduce(upto, spread[:, :, :], AX_X, ALU.add))
            table(V.tensor_scalar(weight, nblk, -float(P), float(REGION), ALU.mult, ALU.add))
            table(V.tensor_scalar(last, upto[:, E - 1:E], -1.0, None, ALU.add))
            table(V.tensor_scalar(b, block_no[:, 0:BLOCKS], last, None, ALU.min))
            table(V.tensor_tensor(p0, over_blocks(upto), b.rearrange("p (b a) -> p b a", a=1)
                                  .broadcast_to([P, BLOCKS, E]), ALU.is_le))
            table(V.tensor_tensor(p1, p0, over_blocks(weight), ALU.mult))
            table(V.tensor_reduce(row, p1, AX_X, ALU.add))
            V.scalar_tensor_tensor(block_row[:, 0:BLOCKS], b, float(P), row, ALU.mult, ALU.add).then_inc(rows_done, 1)
            table(V.tensor_reduce(e_of, p0, AX_X, ALU.add))
            for i in range(4):
                V.tensor_copy(step_experts[:, 4 - i:4 - i + BLOCKS, i], e_of).then_inc(experts_set, 1)
            dve.wait_ge(experts_set, 4)
            table(V.tensor_copy(table8[:, 1, SLOTS:E], upto[:, 0:E - SLOTS]))
            table(V.tensor_copy(table8[:, 1, 0:1], upto[:, E - 2:E - 1]))
            table(sub(ends, upto, nblk))
            table(V.scalar_tensor_tensor(shift, ends, float(P), region_base[:, :], ALU.mult, ALU.subtract))
            table(V.tensor_tensor(hot_delta[:, :, :], hot_all[:, :, :, :].rearrange("p t k e -> p (t k) e"),
                                  shift.rearrange("p (a e) -> p a e", a=1).broadcast_to([P, TILES * TOPK, E]),
                                  ALU.mult))
            at_row = rs[:, 0:2, :].rearrange("p a t -> p (a t)")
            table(V.tensor_reduce(at_row, hot_delta[:, :, :], AX_X, ALU.add))
            table(V.tensor_tensor(ypos_i[:, :, :].rearrange("p t k -> p (t k)"), at_row,
                                  pos_all[:, :, :].rearrange("p t k -> p (t k)"), ALU.add))
            V.memset(table8[:, 1, 1:2], 0).then_inc(tables_done, 1)
            dve.wait_ge(gate_exp, 1)
            table(V.tensor_reduce(gate_s[:, 1, :], gate_e[:, :, :], AX_X, ALU.add))
            table(V.reciprocal(gate_s[:, 2, :], gate_s[:, 1, :]))
            table(V.tensor_tensor(gate_e[:, :, :], gate_e[:, :, :], over_experts(gate_s[:, 2, :]), ALU.mult))
            for k in range(TOPK):
                table(V.tensor_tensor(gate_h[:, :, :], gate_e[:, :, :], hot_all[:, :, k, :], ALU.mult))
                table(V.tensor_reduce(gates[:, k, :], gate_h[:, :, :], AX_X, ALU.add))

            def bias_row(e, p):
                return tile_of(bias[:, :, B_AT[p]:B_AT[p] + B_SIZES[p]], e % B_SLOTS, P)

            def biases_of(e):
                dve.wait_ge(bias_in, 16 * e + 16)

            def experts(s):
                e_y, e_u, e_g, e_h = experts_of(mybir.EngineType.DVE, s)
                if known(s - 1, BLOCKS):
                    wait(dve, u_mm, s)
                    wait(dve, gated_done, s - 1)
                    V.tensor_tensor(vsum[:, :], ps[:, 3, :], bias_row(e_u, 2), ALU.add).then_inc(u_sum, 1)
                    wait(dve, u_sum, s)
                    wait(dve, silu_done, s)
                    wait(dve, gT_mm, s - 1)
                    V.tensor_tensor(gated[:, :], vsum[:, :], silu[:, :], ALU.mult).then_inc(gated_done, 1)
                if known(s, BLOCKS):
                    wait(dve, hT_hi, s + 1)
                    sub(hT[1][:, :, :], ps[:, 0, :].rearrange("p (k n) -> p k n", n=P), r32(hT[0][:, :, :])
                        ).then_inc(hT_lo, 1)
                if known(s - 2, BLOCKS):
                    wait(dve, y_mm, s - 1)
                    wait(dve, y_out, 16 * (s - 2))
                    V.tensor_tensor(yhalf[:, :], ps[:, 5, 0:D], bias_row(e_y, 3), ALU.add).then_inc(y_lower, 1)
                    wait(dve, y_lower, s - 1)
                    V.tensor_tensor(ysum[:, :], ps[:, 5, D:2 * D], yhalf[:, :], ALU.add).then_inc(y_sum, 1)
                if known(s + 1, BLOCKS):
                    biases_of(e_h)
                    wait(dve, h_mm, s + 2)
                    wait(dve, hT_mm, s + 1)
                    V.tensor_tensor(hsum[:, :], ps[:, 1, :], bias_row(e_h, 0), ALU.add).then_inc(h_sum, 1)
                if known(s - 1, BLOCKS):
                    wait(dve, gT_hi, s)
                    sub(gT[1][:, :, :], ps[:, 4, :].rearrange("p (k n) -> p k n", n=P), r32(gT[0][:, :, :])
                        ).then_inc(gT_lo, 1)
                if known(s, BLOCKS):
                    wait(dve, g_mm, s + 1)
                    wait(dve, silu_done, s)
                    V.tensor_tensor(gsum[:, :], ps[:, 2, :], bias_row(e_g, 1), ALU.add).then_inc(g_sum, 1)
                if known(s + 2, BLOCKS):
                    wait(dve, bT_hi, s + 3)
                    sub(bT[1][:, :, :], ps[:, 6, 0:D].rearrange("p (k n) -> p k n", n=P), r32(bT[0][:, :, :])
                        ).then_inc(bT_lo, 1)
            for s in (-2, -1):
                experts(s)
            pipeline(dve, experts, 3, BLOCKS - 2, BLOCKS + 2)

            for k in range(TOPK):
                for t in range(TILES):
                    n = width(t)
                    dve.wait_ge(gathered[t][k], 16)
                    if k:
                        dve.wait_ge(part_added, t + 1)
                    V.scalar_tensor_tensor((x1, result)[k][:n, t, :], picked[:n, t, k, :], gates[:n, k, t:t + 1],
                                           x1[:n, t, :], ALU.mult, ALU.add).then_inc((part_added, added)[k], 1)


_INS = ["x", "adj", "L0_gnn_Wq", "L0_gnn_bq", "L0_gnn_Wk", "L0_gnn_bk", "L0_gnn_Wv", "L0_gnn_bv",
        "L0_ffn_router_w", "L0_ffn_router_b", "L0_ffn_w1", "L0_ffn_b1", "L0_ffn_wg", "L0_ffn_bg",
        "L0_ffn_wv", "L0_ffn_bv", "L0_ffn_w2", "L0_ffn_b2"]


def kernel(**inputs):
    import numpy as np
    import concourse.bacc as bacc
    from concourse.bass_utils import run_bass_kernel_spmd

    nc = bacc.Bacc("TRN2", target_bir_lowering=False, num_devices=1)
    arrays, args = {}, []
    for name in _INS:
        a = np.ascontiguousarray(inputs[name])
        arrays[f"in_{name}"] = a
        args.append(nc.dram_tensor(f"in_{name}", a.shape, mybir.dt.from_np(a.dtype), kind="ExternalInput").ap())
    n, d = inputs["x"].shape
    args.append(nc.dram_tensor("out", (n, d), F32, kind="ExternalOutput").ap())
    attention_then_top2_experts(nc, *args)
    return run_bass_kernel_spmd(nc, [arrays], core_ids=[0]).results[0]["out"]
```
